# Optimizing a Trainium2 kernel written in Bass

```python
import numpy as np
import jax
import jax.numpy as jnp

def _softmax(x, axis=-1):
    return jax.nn.softmax(x, axis=axis)

def _gelu(x):
    return jax.nn.gelu(x, approximate=True)

def _silu(x):
    return jax.nn.silu(x)

def _sigmoid(x):
    return jax.nn.sigmoid(x)

def _layernorm(x, axis=-1, eps=1e-05):
    m = jnp.mean(x, axis=axis, keepdims=True)
    v = jnp.var(x, axis=axis, keepdims=True)
    return (x - m) / jnp.sqrt(v + eps)

def _scatter_add(tgt, idx, src, axis=0):
    return tgt.at[idx].add(src)

def _segment_sum(src, seg, n):
    return jax.ops.segment_sum(src, seg, n)
kernel_name = 'mk_recurrent_d1_jaxref_r2_2a5619'

def setup_inputs(seed: int=0):
    np.random.seed(seed)
    _w = jnp.asarray

    def _L0_attn_setup():
        import jax, jax.numpy as jnp
        import numpy as np
        from jax import lax
        B, T, D, H, K = (2, 1024, 512, 16, 4)
        HD = D // H
        CONV_DIM = 3 * D

        def _l2norm(x, eps=1e-06):
            return x * lax.rsqrt(jnp.sum(x * x, axis=-1, keepdims=True) + eps)

        def _forward(x, W_qkv, conv_w, W_z, W_b, W_a, dt_bias, A_log, W_out):
            b_, t_, d_ = x.shape
            mixed = jnp.einsum('btd,cd->btc', x, W_qkv)
            c = mixed.transpose(0, 2, 1)
            c = lax.conv_general_dilated(c, conv_w, window_strides=(1,), padding=[(K - 1, 0)], dimension_numbers=('NCH', 'OIH', 'NCH'), feature_group_count=CONV_DIM)
            mixed = jax.nn.silu(c).transpose(0, 2, 1)
            q, k, v = jnp.split(mixed, [d_, 2 * d_], axis=-1)
            q = q.reshape(b_, t_, H, HD)
            k = k.reshape(b_, t_, H, HD)
            v = v.reshape(b_, t_, H, HD)
            z = jnp.einsum('btd,ed->bte', x, W_z).reshape(b_, t_, H, HD)
            beta = jax.nn.sigmoid(jnp.einsum('btd,hd->bth', x, W_b))
            g = -jnp.exp(A_log) * jax.nn.softplus(jnp.einsum('btd,hd->bth', x, W_a) + dt_bias)
            q = _l2norm(q) * HD ** (-0.5)
            k = _l2norm(k)
            qs = q.transpose(1, 0, 2, 3)
            ks_ = k.transpose(1, 0, 2, 3)
            vs = v.transpose(1, 0, 2, 3)
            bs = beta.transpose(1, 0, 2)
            gs = g.transpose(1, 0, 2)

            def step(S, inp):
                q_t, k_t, v_t, b_t, g_t = inp
                S = S * jnp.exp(g_t)[..., None, None]
                S = S + jnp.einsum('bhd,bhv->bhdv', k_t, v_t * b_t[..., None])
                o_t = jnp.einsum('bhd,bhdv->bhv', q_t, S)
                return (S, o_t)
            S0 = jnp.zeros((b_, H, HD, HD), x.dtype)
            _, out = lax.scan(step, S0, (qs, ks_, vs, bs, gs))
            out = out.transpose(1, 0, 2, 3)
            var = jnp.mean(out * out, axis=-1, keepdims=True)
            out = out * lax.rsqrt(var + 1e-06) * jax.nn.silu(z)
            out = out.reshape(b_, t_, d_)
            return jnp.einsum('btd,ed->bte', out, W_out)
        key = jax.random.key(seed)
        ks = jax.random.split(key, 8)
        s = 0.02
        return {'x': jax.random.normal(ks[0], (B, T, D), jnp.float32), 'W_qkv': jax.random.normal(ks[1], (CONV_DIM, D), jnp.float32) * s, 'conv_w': jax.random.normal(ks[2], (CONV_DIM, 1, K), jnp.float32) * 0.25, 'W_z': jax.random.normal(ks[3], (D, D), jnp.float32) * s, 'W_b': jax.random.normal(ks[4], (H, D), jnp.float32) * s, 'W_a': jax.random.normal(ks[5], (H, D), jnp.float32) * s, 'dt_bias': jnp.ones((H,), jnp.float32), 'A_log': jnp.log(jnp.arange(1, H + 1, dtype=jnp.float32)), 'W_out': jax.random.normal(ks[6], (D, D), jnp.float32) * s}
    _L0_attn_in = _L0_attn_setup()

    def _L0_ffn_setup():
        import jax, jax.numpy as jnp
        import numpy as np
        HIDDEN = 512
        FF = 2048
        N_EXPERTS = 8
        CAP_FACTOR = 1.0
        B, S = (4, 1024)
        STD = 0.02

        def _gelu(x):
            return x * 0.5 * (1.0 + jax.lax.erf(x / 1.41421))
        key = jax.random.key(seed)
        ks = jax.random.split(key, 6)
        x = jax.random.normal(ks[0], (B, S, HIDDEN), dtype=jnp.float32)
        W_sw = jax.random.normal(ks[1], (HIDDEN, N_EXPERTS), dtype=jnp.float32) * STD
        b_sw = jnp.zeros((N_EXPERTS,), dtype=jnp.float32)
        W1 = jax.random.normal(ks[2], (N_EXPERTS, HIDDEN, FF), dtype=jnp.float32) * STD
        b1 = jnp.zeros((N_EXPERTS, FF), dtype=jnp.float32)
        W2 = jax.random.normal(ks[3], (N_EXPERTS, FF, HIDDEN), dtype=jnp.float32) * STD
        b2 = jnp.zeros((N_EXPERTS, HIDDEN), dtype=jnp.float32)
        return {'x': x, 'W_sw': W_sw, 'b_sw': b_sw, 'W1': W1, 'b1': b1, 'W2': W2, 'b2': b2}
    _L0_ffn_in = _L0_ffn_setup()
    _d = {'L0_attn_x': _L0_attn_in['x'], 'L0_attn_W_qkv': _L0_attn_in['W_qkv'], 'L0_attn_conv_w': _L0_attn_in['conv_w'], 'L0_attn_W_z': _L0_attn_in['W_z'], 'L0_attn_W_b': _L0_attn_in['W_b'], 'L0_attn_W_a': _L0_attn_in['W_a'], 'L0_attn_dt_bias': _L0_attn_in['dt_bias'], 'L0_attn_A_log': _L0_attn_in['A_log'], 'L0_attn_W_out': _L0_attn_in['W_out'], 'L0_ffn_W_sw': _L0_ffn_in['W_sw'], 'L0_ffn_b_sw': _L0_ffn_in['b_sw'], 'L0_ffn_W1': _L0_ffn_in['W1'], 'L0_ffn_b1': _L0_ffn_in['b1'], 'L0_ffn_W2': _L0_ffn_in['W2'], 'L0_ffn_b2': _L0_ffn_in['b2']}
    _x0 = _d['L0_attn_x']
    _d['L0_attn_x'] = jax.random.normal(jax.random.fold_in(jax.random.key(seed), 1), (4, 2048, 512), dtype=_x0.dtype)
    del _x0
    return _d

def reference(L0_attn_x, L0_attn_W_qkv, L0_attn_conv_w, L0_attn_W_z, L0_attn_W_b, L0_attn_W_a, L0_attn_dt_bias, L0_attn_A_log, L0_attn_W_out, L0_ffn_W_sw, L0_ffn_b_sw, L0_ffn_W1, L0_ffn_b1, L0_ffn_W2, L0_ffn_b2):

    def _L0_attn_ref(x, W_qkv, conv_w, W_z, W_b, W_a, dt_bias, A_log, W_out):
        import jax, jax.numpy as jnp
        import numpy as np
        from jax import lax
        B, T, D, H, K = (2, 1024, 512, 16, 4)
        HD = D // H
        CONV_DIM = 3 * D

        def _l2norm(x, eps=1e-06):
            return x * lax.rsqrt(jnp.sum(x * x, axis=-1, keepdims=True) + eps)

        def _forward(x, W_qkv, conv_w, W_z, W_b, W_a, dt_bias, A_log, W_out):
            b_, t_, d_ = x.shape
            mixed = jnp.einsum('btd,cd->btc', x, W_qkv)
            c = mixed.transpose(0, 2, 1)
            c = lax.conv_general_dilated(c, conv_w, window_strides=(1,), padding=[(K - 1, 0)], dimension_numbers=('NCH', 'OIH', 'NCH'), feature_group_count=CONV_DIM)
            mixed = jax.nn.silu(c).transpose(0, 2, 1)
            q, k, v = jnp.split(mixed, [d_, 2 * d_], axis=-1)
            q = q.reshape(b_, t_, H, HD)
            k = k.reshape(b_, t_, H, HD)
            v = v.reshape(b_, t_, H, HD)
            z = jnp.einsum('btd,ed->bte', x, W_z).reshape(b_, t_, H, HD)
            beta = jax.nn.sigmoid(jnp.einsum('btd,hd->bth', x, W_b))
            g = -jnp.exp(A_log) * jax.nn.softplus(jnp.einsum('btd,hd->bth', x, W_a) + dt_bias)
            q = _l2norm(q) * HD ** (-0.5)
            k = _l2norm(k)
            qs = q.transpose(1, 0, 2, 3)
            ks_ = k.transpose(1, 0, 2, 3)
            vs = v.transpose(1, 0, 2, 3)
            bs = beta.transpose(1, 0, 2)
            gs = g.transpose(1, 0, 2)

            def step(S, inp):
                q_t, k_t, v_t, b_t, g_t = inp
                S = S * jnp.exp(g_t)[..., None, None]
                S = S + jnp.einsum('bhd,bhv->bhdv', k_t, v_t * b_t[..., None])
                o_t = jnp.einsum('bhd,bhdv->bhv', q_t, S)
                return (S, o_t)
            S0 = jnp.zeros((b_, H, HD, HD), x.dtype)
            _, out = lax.scan(step, S0, (qs, ks_, vs, bs, gs))
            out = out.transpose(1, 0, 2, 3)
            var = jnp.mean(out * out, axis=-1, keepdims=True)
            out = out * lax.rsqrt(var + 1e-06) * jax.nn.silu(z)
            out = out.reshape(b_, t_, d_)
            return jnp.einsum('btd,ed->bte', out, W_out)
        return _forward(x, W_qkv, conv_w, W_z, W_b, W_a, dt_bias, A_log, W_out)

    def _L0_ffn_ref(x, W_sw, b_sw, W1, b1, W2, b2):
        import jax, jax.numpy as jnp
        import numpy as np
        HIDDEN = 512
        FF = 2048
        N_EXPERTS = 8
        CAP_FACTOR = 1.0
        B, S = (4, 1024)
        STD = 0.02

        def _gelu(x):
            return x * 0.5 * (1.0 + jax.lax.erf(x / 1.41421))
        Bb, Ss, D = x.shape
        T = Bb * Ss
        E = W1.shape[0]
        capacity = int(CAP_FACTOR * T / E)
        xf = x.reshape(T, D)
        logits = xf @ W_sw + b_sw
        probs = jax.nn.softmax(logits, axis=-1)
        pmax = jnp.max(probs, axis=-1)
        routes = jnp.argmax(probs, axis=-1)
        factor = pmax / jax.lax.stop_gradient(pmax)
        xs = xf * factor[:, None]
        onehot = jax.nn.one_hot(routes, E, dtype=jnp.int32)
        pos = jnp.cumsum(onehot, axis=0) - 1
        pos_tok = jnp.take_along_axis(pos, routes[:, None], axis=1)[:, 0]
        keep = pos_tok < capacity
        pos_safe = jnp.where(keep, pos_tok, capacity)
        buf = jnp.zeros((E, capacity + 1, D), dtype=xs.dtype)
        buf = buf.at[routes, pos_safe].set(xs)
        buf = buf[:, :capacity]
        h = _gelu(jnp.einsum('ecd,edf->ecf', buf, W1) + b1[:, None, :])
        expert_out = jnp.einsum('ecf,efd->ecd', h, W2) + b2[:, None, :]
        gathered = expert_out[routes, jnp.minimum(pos_tok, capacity - 1)]
        final = jnp.where(keep[:, None], gathered, xs)
        return final.reshape(Bb, Ss, D)
    x = L0_attn_x
    xn = _layernorm(x, axis=-1)
    s = _L0_attn_ref(xn, L0_attn_W_qkv, L0_attn_conv_w, L0_attn_W_z, L0_attn_W_b, L0_attn_W_a, L0_attn_dt_bias, L0_attn_A_log, L0_attn_W_out)
    g = _silu(_L0_ffn_ref(xn, L0_ffn_W_sw, L0_ffn_b_sw, L0_ffn_W1, L0_ffn_b1, L0_ffn_W2, L0_ffn_b2))
    x = x + s * g
    return x

_drawn_inputs = setup_inputs


def setup_inputs(seed=0):
    import zlib

    import numpy as np

    out = dict(_drawn_inputs(seed))
    spreads = {'L0_attn_dt_bias': (1.0, 0.6),
     'L0_ffn_b_sw': (0.0, 0.38),
     'L0_ffn_b1': (0.0, 0.8),
     'L0_ffn_b2': (0.0, 0.8)}
    factors = {'L0_attn_W_b': 8.0,
     'L0_attn_W_a': 8.0,
     'L0_attn_A_log': 8.0,
     'L0_ffn_W_sw': 3.446,
     'L0_ffn_W1': 7.063,
     'L0_ffn_W2': 6.601}
    for name, (base, spread) in spreads.items():
        noise = np.random.default_rng([zlib.crc32(name.encode()), seed]).standard_normal(out[name].shape)
        drawn = base * np.exp(spread * noise) if base else spread * noise
        out[name] = jnp.asarray(drawn.astype(out[name].dtype))
    for name, factor in factors.items():
        out[name] = (out[name] * factor).astype(out[name].dtype)
    return out
```

```python
from contextlib import ExitStack

import concourse.bass as bass
from concourse import mybir
from concourse.alu_op_type import AluOpType as ALU

ACT = mybir.ActivationFunctionType
F32 = mybir.dt.float32
F32R = mybir.dt.float32r
BF16 = mybir.dt.bfloat16
I32 = mybir.dt.int32
U32 = mybir.dt.uint32
AX = mybir.AxisListType

P = 128
GELU_R = 2.0 ** 0.5 / 1.41421


STAGES = [
    ("stats", 0), ("kT", 0), ("decay_cm", 0), ("rms", "prev"), ("z", 0), ("ss", 0), ("k_sum", 0), ("late_conv", 5), ("norms", 0),
    ("silu_z", 0), ("late_silu", 5),
    ("tile", 0, 0), ("xn", 0), ("z", 1), ("silu_z", 1), ("vT", 0), ("vp", 0), ("og", "prev"),
    ("tile", 0, 1), ("oT", "prev"), ("oHi", "prev"), ("oLo", "prev"), ("xT", 0),
    ("tile", 0, 2), ("out", "prev"), ("gates", 0), ("unit", 0), ("pre", 0), ("squares", 1), ("route", 0),
    ("tile", 0, 3), ("vw", 0), ("qblocks", 1), ("unit", 1), ("pre", 1), ("softplus", 0),
    ("finish", 0), ("decay_cm", 1), ("conv", 0), ("unit", 2), ("kT", 1), ("pre", 2), ("factor", 0),
    ("ss", 1), ("rms", 0), ("k_sum", 1), ("conv", 1), ("norms", 1), ("vT", 1), ("vp", 1), ("og", 0), ("silu", 0), ("silu", 1),
    ("unit", 3), ("pre", 3),
    ("tile", 1, 0), ("unit", 4), ("oT", 0), ("oHi", 0), ("oLo", 0),
    ("tile", 1, 1), ("conv", 2), ("silu", 2), ("pre", 4), ("e_split", 0), ("out", 0),
    ("tile", 1, 2), ("conv", 3), ("silu", 3), ("next_squares", 0), ("unit", 5), ("decays", 0),
    ("tile", 1, 3), ("vw", 1), ("turned_decays", 0), ("pre", 5), ("next_qblocks", 0), ("conv", 4), ("silu", 4),
    ("finish", 1),
]
NEXT = {"stats", "xn", "xT", "gates", "route", "factor", "softplus", "e_split", "decays", "turned_decays", "unit", "pre", "conv", "silu",
        "next_squares", "next_qblocks"}
FRONT = [s for s in STAGES if s[0] in NEXT]
FIRST = [s for s in STAGES if s[1] != "prev"]
LAST = [s for s in STAGES if s[0] not in NEXT]
TAIL = [s for s in STAGES if s[1] == "prev"]
XBANKS = ["m0", "kv"]
BANKS = ["pj0", "pj1", "eb", "sc", "o", "kv", "m0", "m1"]


def fills_of(stage):
    kind, c = stage[0], stage[1]
    return {
        "kT": [("m0", f"kT{c}")],
        "ss": [("kv", f"ss{c}")],
        "vT": [("m1", f"vT{c}")],
        "z": [(f"pj{c}", f"z{c}")] if kind == "z" else [],
        "decay_cm": [("eb", f"cd{c}")],
        "tile": [("eb", f"e{stage[1:]}"), ("sc", f"s{stage[1:]}")],
        "xT": [("m0", "x0"), ("kv", "x1")],
        "gates": [("m0", "g")],
        "route": [("m0", "r")],
        "decays": [("m0", "e")],
        "oT": [("m1", f"oT{c}")],
        "out": [("m1", f"out{c}")],
        "unit": [(f"pj{c % 2}", f"u{c}")] if kind == "unit" else [],
        "finish": [("o", f"o{c}"), ("kv", f"kv{c}")],
    }.get(kind, [])


def names_in(stages, bank):
    return [name for st in stages for b, name in fills_of(st) if b == bank]


class Step:

    def __init__(self, n, half, parity, stages, groups):
        self.n, self.half, self.parity, self.stages = n, half, parity, stages
        self.base = {}
        for b in BANKS:
            pro, first, whole, last = (len(names_in(s, b)) for s in (FRONT, FIRST, STAGES, LAST))
            if stages is FRONT:
                self.base[b] = 0
            elif stages is FIRST:
                self.base[b] = pro
            elif stages is TAIL:
                self.base[b] = pro + first + whole * (groups - 2) + last
            else:
                self.base[b] = whole * (n - 1) + (pro + first)

    def fill(self, bank, name):
        return self.base[bank] + (names_in(self.stages, bank).index(name) + 1)

    def chunk(self, c):
        return 2 * self.n + (-1 if c == "prev" else c)


def steps_of(eng, groups, body, ahead=0):
    body(Step(-1, -1, 1, FRONT, groups))
    body(Step(0, 0, 0, FIRST, groups))
    pairs = (groups - 2 - ahead) // 2
    with eng.Fori(0, pairs) as i:
        body(Step(2 * i + 1, i, 1, STAGES, groups))
        body(Step(2 * i + 2, i + 1, 0, STAGES, groups))
    for n in range(2 * pairs + 1, groups - 1):
        body(Step(n, n // 2, n % 2, STAGES, groups))
    body(Step(groups - 1, (groups - 1) // 2, 1, LAST, groups))
    body(Step(groups, groups // 2, 0, TAIL, groups))




def after(eng, semaphore, count):
    if not (isinstance(count, int) and count <= 0):
        eng.wait_ge(semaphore, count)


def row(ap, i):
    return ap[i] if isinstance(i, int) else ap[bass.ds(i, 1)].squeeze(0)


def column(ap, i):
    return ap[:, i:i + 1] if isinstance(i, int) else ap[:, bass.ds(i, 1)]


def build(nc, x, W_qkv, conv_w, W_z, W_b, W_a, dt_bias, A_log, W_out, W_sw, b_sw, W1, b1, W2, b2, out):
    xf = x.rearrange("b t d -> (b t) d")
    outf = out.rearrange("b t d -> (b t) d")
    NTOK, D = xf.shape
    xs_tab = nc.dram_tensor("xs_tab", [NTOK, D], F32, kind="Internal").ap()
    s_tab = nc.dram_tensor("s_tab", [NTOK, D], F32, kind="Internal").ap()
    tok_tab = nc.dram_tensor("tok_tab", [NTOK, 1], I32, kind="Internal").ap()
    with ExitStack() as top:
        bank = {b: top.enter_context(nc.psum_tensor(f"bank_{b}", [P, 512], F32)) for b in BANKS}
        ident = top.enter_context(nc.sbuf_tensor("ident", [P, P], F32))
        with ExitStack() as ctx:
            phase_a(nc, ctx, bank, ident, xf, outf, xs_tab, s_tab, tok_tab, W_qkv, conv_w, W_z, W_b, W_a,
                    dt_bias, A_log, W_out, W_sw, b_sw, x.shape[1])
        with ExitStack() as ctx:
            phase_b(nc, ctx, bank, ident, xf, outf, xs_tab, s_tab, tok_tab, W1, b1, W2, b2)


def phase_a(nc, ctx, bank, ident, xf, outf, xs_tab, s_tab, tok_tab, W_qkv, conv_w, W_z, W_b, W_a,
            dt_bias, A_log, W_out, W_sw, b_sw, T):
    NTOK, D = xf.shape
    C3, (H, _), E = W_qkv.shape[0], W_b.shape, W_sw.shape[1]
    HD = D // H
    CAP = NTOK // E
    GT = 2 * P
    GROUPS = NTOK // GT
    PER_BATCH = T // GT
    KC = D // P
    NCT = C3 // P
    QT = D // P
    HPT = P // HD
    NG = E + 2 * H
    WCOLS = C3 + 2 * D
    NU = NCT // 2
    NO_TOKEN = 1 << 20
    x_g = xf.rearrange("(g t p) d -> g p t d", p=P, t=2)
    xs_g = xs_tab.rearrange("(g t p) d -> g p t d", p=P, t=2)
    x_q, s_q, out_q = (a.rearrange("(q p) d -> q p d", p=P) for a in (xf, s_tab, outf))

    def sb(name, shape, dt=F32):
        return ctx.enter_context(nc.sbuf_tensor(name, shape, dt))

    def sem(name):
        return ctx.enter_context(nc.semaphore(name))

    ident4 = sb("ident4", [P, HPT * P])
    tri = sb("tri", [P, P], BF16)
    ones = sb("ones", [P, P], BF16)
    bdmask = sb("bdmask", [P, P])
    headsum = sb("headsum", [P, HPT])
    zeros = sb("zeros", [P, P])
    ind = sb("ind", [32, H])
    ind_r = sb("ind_r", [32, H], F32R)
    ind_cm = sb("ind_cm", [32, D], F32R)
    keep_first = sb("keep_first", [P, GROUPS])
    keep_halo = sb("keep_halo", [P, GROUPS])
    eidx = sb("eidx", [P, E])
    eps_ln = sb("eps_ln", [P, 1])
    eps_n = sb("eps_n", [P, 1])
    negA = sb("negA", [P, H])
    bias_row = sb("bias_row", [P, NG])
    cw = sb("cw", [P, NCT, 4])
    wT_hi = sb("wT_hi", [P, KC, WCOLS], F32R)
    wT_lo = sb("wT_lo", [P, KC, WCOLS], F32R)
    wg = sb("wg", [P, KC, NG])
    wg_hl = sb("wg_hl", [P, KC, 2, NG], F32R)
    no_token = sb("no_token", [P, NTOK // P], I32)
    xin = [sb(f"xin{i}", [P, 2, D]) for i in range(2)]
    xn = sb("xn", [P, 2, D])
    xs = [sb(f"xs{i}", [P, 2, D]) for i in range(2)]
    xT_hi = sb("xT_hi", [P, KC, GT], F32R)
    xT_lo = sb("xT_lo", [P, KC, GT], F32R)
    pre = [sb(f"pre{i}", [P, 2, GT + 3]) for i in range(2)]
    tap0 = [sb(f"tap0_{i}", [P, 2, GT]) for i in range(2)]
    halo = sb("halo", [P, NCT, 3])
    qkv = [sb(f"qkv{i}", [P, NCT, GT]) for i in range(2)]
    sz = sb("sz", [P, 2, D])
    bn = sb("bn", [P, 2, 6])
    mv = sb("mv", [P, 2, 2])
    ln_sd = sb("ln_sd", [P, 2])
    rstd = sb("rstd", [P, 2])
    nmr = sb("nmr", [P, 2])
    gl = sb("gl", [P, 2, NG])
    mx = sb("mx", [P, 2])
    eq = sb("eq", [P, 2, E])
    cand = sb("cand", [P, 2, E])
    rid = sb("rid", [P, 2])
    oh = sb("oh", [P, 2, E], BF16)
    count = sb("count", [P, E])
    rank = sb("rank", [P, 2, E])
    pos = sb("pos", [P, 2])
    over = sb("over", [P, 2])
    slot_f = sb("slot_f", [P, 2])
    slot = [sb(f"slot{i}", [P, 2], I32) for i in range(2)]
    tok_f = sb("tok_f", [P, 2])
    tok = [sb(f"tok{i}", [P, 2], I32) for i in range(2)]
    lsub = sb("lsub", [P, 2, E])
    lexp = sb("lexp", [P, 2, E])
    lsum = sb("lsum", [P, 2])
    pmax = sb("pmax", [P, 2])
    rpmax = sb("rpmax", [P, 2])
    factor = sb("factor", [P, 2])
    beta = [sb(f"beta{i}", [P, 2, H]) for i in range(2)]
    bexp = sb("bexp", [P, 2, H])
    aabs = sb("aabs", [P, 2, H])
    yexp = sb("yexp", [P, 2, H])
    yden = sb("yden", [P, 2, H])
    sat = sb("sat", [P, 2, H])
    sat2 = sb("sat2", [P, 2, H])
    poly = sb("poly", [P, 2, H])
    dec = sb("dec", [P, 2, H])
    e_raw = sb("e_raw", [P, 2, H])
    e_hl = sb("e_hl", [P, 2, 2, H], F32R)
    eT = [sb(f"eT{i}", [32, 2, P], F32R) for i in range(2)]
    eTz = [sb(f"eTz{i}", [32, 2, P], F32R) for i in range(2)]
    sq = sb("sq", [P, QT, P])
    ksq = sb("ksq", [P, D])
    kss = sb("kss", [P, H])
    nsd = sb("nsd", [P, 2 * H])
    rqk = sb("rqk", [P, 2 * H])
    vscale = sb("vscale", [P, H])
    k_tm = sb("k_tm", [P, D])
    vp = sb("vp", [P, D])
    vw = sb("vw", [P, D])
    wlast = sb("wlast", [P, H])
    cdT = sb("cdT", [P, QT, P])
    cdlast = [sb(f"cdlast{i}", [P, QT]) for i in range(2)]
    qd = sb("qd", [P, QT, P])
    qbd = sb("qbd", [P, QT, HPT, P])
    dm = [sb(f"dm{i}", [P, HPT * P]) for i in range(2)]
    pm = [sb(f"pm{i}", [P, HPT * P]) for i in range(2)]
    state = sb("state", [P, QT, P])
    kvm = vw[:, :].rearrange("p (t v) -> p t v", t=QT)
    o1 = sb("o1", [P, D])
    oz = o1
    og = sb("og", [P, D])
    osq = og
    ovar = sb("ovar", [P, H])
    osd = sb("osd", [P, H])
    orn = sb("orn", [P, H])
    oT_hi = sb("oT_hi", [P, KC, P], F32R)
    oT_lo = sb("oT_lo", [P, KC, P], F32R)
    s_sb = sb("s_sb", [P, D])
    fd = sb("fd", [P, D])
    xr = sb("xr", [P, D])
    ob = fd

    filled = {b: sem(f"{b}_filled") for b in BANKS}
    emptied = {b: sem(f"{b}_emptied") for b in BANKS}
    rows_staged = [sem(f"rows_staged{i}") for i in range(4)]
    (const_ready, rows_turned, wT_hi_ready, wT_lo_ready, small_loaded, gate_rows_loaded,
     gate_turned, wg_step, negA_ready, tok_cleared, const_made) = (sem(n) for n in (
         "const_ready rows_turned wT_hi_ready wT_lo_ready small_loaded gate_rows_loaded "
         "gate_turned wg_step negA_ready tok_cleared const_made").split())
    x_loaded = [sem(f"x_loaded{i}") for i in range(2)]
    xs_stored = [sem(f"xs_stored{i}") for i in range(2)]
    tok_scattered = [sem(f"tok_scattered{i}") for i in range(2)]
    (bn_ready, mv_ready, ln_sd_ready, rstd_ready, nmr_ready, xn_ready, xT_hi_ready, gl_ready, route_step, slot_ready,
     lexp_ready, bexp_ready, yexp_ready, factor_step, xs_ready, tok_step,
     soft_step, e_raw_ready, e_step, eTz_step, halo_in, halo_saved, tap_ready, first_tap_ready, conv_step, qkv_ready) = (
         sem(n) for n in (
             "bn_ready mv_ready ln_sd_ready rstd_ready nmr_ready xn_ready xT_hi_ready gl_ready route_step slot_ready "
             "lexp_ready bexp_ready yexp_ready factor_step xs_ready tok_step "
             "soft_step e_raw_ready e_step eTz_step halo_in halo_saved tap_ready first_tap_ready conv_step qkv_ready").split())
    (sq_ready, ksq_ready, kss_ready, ksd_ready, rqk_ready, vscale_ready, qbd_ready, qd_ready, cdlast_ready, wlast_ready, weighed, vw_ready,
     state_decayed, state_ready, osq_ready, ovar_ready, osd_ready, orn_ready, oz_ready, og_ready,
     oT_hi_ready, fd_ready, xr_loaded, s_stored, ob_step, ob_ready, ob_stored) = (sem(n) for n in (
         "sq_ready ksq_ready kss_ready ksd_ready rqk_ready vscale_ready qbd_ready qd_ready cdlast_ready wlast_ready weighed vw_ready "
         "state_decayed state_ready osq_ready ovar_ready osd_ready orn_ready oz_ready og_ready "
         "oT_hi_ready fd_ready xr_loaded s_stored ob_step ob_ready ob_stored").split())

    ROWS = [W_qkv[i * P:(i + 1) * P, :] for i in range(NCT)]
    ROWS += [W_z[i * P:(i + 1) * P, :] for i in range(QT)] + [W_out[i * P:(i + 1) * P, :] for i in range(QT)]
    POLY = [0.25 ** k / (2 * k + 1) for k in range(1, 9)]
    ROUTE, FACTOR, SOFT = 13, 5, 9 + len(POLY)
    LOGITS, BCOL, ACOL = slice(0, E), slice(E, E + H), slice(E + H, NG)

    POOL_TAPS = (0, 1, 5)

    def first_taps(n, c):
        return len(POOL_TAPS) * n + sum(i <= c for i in POOL_TAPS)

    def taps(n, c):
        return 2 * (NU + len(POOL_TAPS)) * n + 2 * (c + 1) + 2 * sum(i <= c for i in POOL_TAPS)

    def heads(ap):
        return ap.rearrange("p (h d) -> p h d", d=HD)

    pool_held, sp_held, dve_held = sem("pool_held"), sem("sp_held"), sem("dve_held")
    block = ctx.enter_context(nc.Block())

    @block.sync
    def _(sp):
        for dst, src in ((bias_row[:, LOGITS], b_sw), (bias_row[:, ACOL], dt_bias), (negA[:, :], A_log)):
            sp.dma_start(dst, src.rearrange("(a e) -> a e", a=1).partition_broadcast(P)).then_inc(small_loaded, 16)
        sp.dma_start(cw[:, :, :], conv_w.rearrange("(c p) o k -> p c (o k)", p=P)).then_inc(small_loaded, 16)
        sp.dma_start(wg[:, :, LOGITS], W_sw.rearrange("(k p) e -> p k e", p=P)).then_inc(gate_rows_loaded, 16)
        sp.dma_start(k_tm[0:H, :], W_b).then_inc(gate_rows_loaded, 16)
        sp.dma_start(k_tm[H:2 * H, :], W_a).then_inc(gate_rows_loaded, 16)
        for i, rows in enumerate(ROWS):
            after(sp, rows_turned, i - 3)
            sp.dma_start(xin[i % 2][:, (i // 2) % 2, :], rows).then_inc(rows_staged[i % 4], 16)
        sp.wait_ge(rows_turned, len(ROWS))
        sp.dma_start(xin[0][:, :, :], x_g[0]).then_inc(x_loaded[0], 16)
        sp.dma_start(xin[1][:, :, :], x_g[1]).then_inc(x_loaded[1], 16)
        sp.wait_ge(const_ready, 1)
        sp.dma_start(tok_tab.rearrange("(p c) o -> p (c o)", p=P), no_token[:, :]).then_inc(tok_cleared, 16)

        def body(g):
            nxt = 1 - g.parity
            beyond = isinstance(g.n, int) and g.n + 2 >= GROUPS
            for st in g.stages:
                kind, c = st[0], st[1]
                if kind == "xn" and g.stages is not FRONT and not beyond:
                    sp.wait_ge(xn_ready, 2 * (g.n + 1))
                    sp.sem_inc(sp_held, 1)
                    sp.dma_start(xin[g.parity][:, :, :], row(x_g, g.n + 2)).then_inc(x_loaded[g.parity], 16)
                elif kind == "factor":
                    sp.wait_ge(xs_ready, 2 * (g.n + 2))
                    sp.sem_inc(sp_held, 1)
                    sp.dma_start(row(xs_g, g.n + 1), xs[nxt][:, :, :]).then_inc(xs_stored[nxt], 16)
                elif kind == "out":
                    q = g.chunk(c)
                    after(sp, ob_ready, q)
                    sp.sem_inc(sp_held, 1)
                    sp.dma_start(xr[:, :], row(x_q, q)).then_inc(xr_loaded, 16)
                    sp.wait_ge(emptied["m1"], g.fill("m1", f"out{c}"))
                    sp.sem_inc(sp_held, 1)
                    sp.dma_start(row(s_q, q), s_sb[:, :]).then_inc(s_stored, 16)
                    sp.wait_ge(ob_ready, q + 1)
                    sp.sem_inc(sp_held, 1)
                    sp.dma_start(row(out_q, q), ob[:, :]).then_inc(ob_stored, 16)

        steps_of(sp, GROUPS, body, ahead=2)
        sp.wait_ge(tok_cleared, 16)
        for i in range(2):
            sp.wait_ge(xs_stored[i], 16 * (GROUPS // 2))
        sp.wait_ge(s_stored, 16 * 2 * GROUPS)
        sp.wait_ge(ob_stored, 16 * 2 * GROUPS)

    @block.tensor
    def _(pe):
        def split3(dst, pairs):
            for i, ((ah, al), (bh, bl)) in enumerate(pairs):
                pe.matmul(dst, ah, bh, start=i == 0, stop=False)
                pe.matmul(dst, ah, bl, start=False, stop=False)
                mm = pe.matmul(dst, al, bh, start=False, stop=i == len(pairs) - 1)
            return mm

        def open_bank(g, b, name):
            after(pe, emptied[b], g.fill(b, name) - 1)

        pe.wait_ge(const_made, 2)
        for i in range(len(ROWS)):
            pe.wait_ge(rows_staged[i % 4], 16 * (i // 4 + 1))
            after(pe, wT_lo_ready, i - 1)
            for k in range(KC):
                mm = pe.transpose(bank[f"m{i % 2}"][:, k * P:(k + 1) * P],
                                  xin[i % 2][:, (i // 2) % 2, k * P:(k + 1) * P], ident[:, :])
            mm.then_inc(rows_turned, 1)
        pe.wait_ge(gate_rows_loaded, 48)
        for k in range(KC):
            mm = pe.transpose(bank["eb"][:, k * 2 * H:(k + 1) * 2 * H], k_tm[0:2 * H, k * P:(k + 1) * P], ident[0:2 * H, 0:2 * H])
        mm.then_inc(gate_turned, 1)
        pe.wait_ge(const_ready, 1)
        pe.wait_ge(wg_step, 3)
        pe.wait_ge(wT_lo_ready, len(ROWS))

        def weigh(g, c, t):
            q = g.chunk(c)
            if t == 0:
                open_bank(g, "o", f"o{c}")
                pe.wait_ge(emptied["m1"], g.fill("m1", f"vT{c}"))
            pe.wait_ge(emptied["sc"], g.fill("sc", f"s{(c, t)}"))
            for h in range(HPT):
                col = slice((t * HPT + h) * HD, (t * HPT + h + 1) * HD)
                mm = pe.matmul(bank["o"][:, col], pm[t % 2][:, h * P:(h + 1) * P], vp[:, col],
                               start=(t == 0 and h == 0), stop=False, skip_group_check=True)
            mm.then_inc(weighed, 1)

        def body(g):
            cur = qkv[g.parity]
            for st in g.stages:
                kind, c = st[0], st[1]
                if kind == "kT":
                    cols = slice(c * P, (c + 1) * P)
                    open_bank(g, "m0", f"kT{c}")
                    pe.wait_ge(qkv_ready, NU * g.n + 4)
                    for k in range(QT):
                        mm = pe.transpose(bank["m0"][:, k * P:(k + 1) * P], cur[:, QT + k, cols], ident[:, :])
                    mm.then_inc(filled["m0"], 1)
                elif kind == "ss":
                    open_bank(g, "kv", f"ss{c}")
                    pe.wait_ge(sq_ready, g.chunk(c) + 1)
                    for k in range(QT):
                        mm = pe.matmul(bank["kv"][:, k * HPT:(k + 1) * HPT], sq[:, k, :], headsum[:, :], start=True, stop=True)
                    mm.then_inc(filled["kv"], 1)
                elif kind == "vT":
                    open_bank(g, "m1", f"vT{c}")
                    pe.wait_ge(qkv_ready, NU * g.n + NU)
                    for k in range(QT):
                        mm = pe.transpose(bank["m1"][:, k * P:(k + 1) * P], cur[:, 2 * QT + k, c * P:(c + 1) * P], ident[:, :])
                    mm.then_inc(filled["m1"], 1)
                elif kind == "decay_cm":
                    open_bank(g, "eb", f"cd{c}")
                    pe.wait_ge(eTz_step, 2 * (g.n + 1))
                    for k in range(QT):
                        mm = pe.matmul(bank["eb"][:, k * P:(k + 1) * P], ind_cm[:, k * P:(k + 1) * P], eT[g.parity][:, c, :], start=True, stop=True)
                    mm.then_inc(filled["eb"], 1)
                elif kind == "tile":
                    t = st[2]
                    open_bank(g, "eb", f"e{st[1:]}")
                    for h in range(HPT):
                        lhs = ind_r[:, t * HPT + h:t * HPT + h + 1].to_broadcast([32, P])
                        mm = pe.matmul(bank["eb"][:, h * P:(h + 1) * P], lhs, eTz[g.parity][:, c, :], start=True, stop=True)
                    mm.then_inc(filled["eb"], 1)
                    open_bank(g, "sc", f"s{st[1:]}")
                    pe.wait_ge(qbd_ready, HPT * (g.chunk(c) + 1))
                    pe.matmul(bank["sc"][:, :], cur[:, QT + t, c * P:(c + 1) * P], qbd[:, t, :, :].rearrange("p h i -> p (h i)"),
                              start=True, stop=True).then_inc(filled["sc"], 1)
                    if t > 0:
                        weigh(g, c, t - 1)
                elif kind == "finish":
                    weigh(g, c, QT - 1)
                    pe.wait_ge(qd_ready, g.chunk(c) + 1)
                    pe.wait_ge(state_ready, g.chunk(c) + 1)
                    for t in range(QT):
                        mm = pe.matmul(bank["o"][:, t * P:(t + 1) * P], qd[:, t, :], state[:, t, :], start=False, stop=t == QT - 1, skip_group_check=True)
                    mm.then_inc(filled["o"], 1)
                    open_bank(g, "kv", f"kv{c}")
                    pe.wait_ge(vw_ready, g.chunk(c) + 1)
                    pe.wait_ge(emptied["m0"], g.fill("m0", f"kT{c}"))
                    for t in range(QT):
                        mm = pe.matmul(bank["kv"][:, t * P:(t + 1) * P], k_tm[:, t * P:(t + 1) * P], vw[:, t * P:(t + 1) * P], start=True, stop=True)
                    mm.then_inc(filled["kv"], 1)
                elif kind == "xT":
                    pe.wait_ge(xn_ready, 2 * (g.n + 2))
                    for b, at in enumerate(XBANKS):
                        open_bank(g, at, f"x{b}")
                        for j in range(4):
                            k, t = 2 * b + j // 2, j % 2
                            mm = pe.transpose(bank[at][:, j * P:(j + 1) * P], xn[:, t, k * P:(k + 1) * P], ident[:, :])
                        mm.then_inc(filled[at], 1)
                elif kind == "gates":
                    open_bank(g, "m0", "g")
                    pe.wait_ge(emptied["kv"], g.fill("kv", "x1"))
                    for t in range(2):
                        dst = bank["m0"][:, 2 * t * NG:2 * (t + 1) * NG]
                        tk = slice(t * P, (t + 1) * P)
                        for k in range(KC):
                            for j, a in enumerate((xT_hi, xT_lo)):
                                mm = pe.matmul(dst, a[:, k, tk], wg_hl[:, k, :, :].rearrange("p a c -> p (a c)"),
                                               start=(k == 0 and j == 0), stop=(k == KC - 1 and j == 1))
                    mm.then_inc(filled["m0"], 1)
                elif kind == "route":
                    open_bank(g, "m0", "r")
                    pe.wait_ge(route_step, ROUTE * (g.n + 1) + 6)
                    flat = oh[:, :, :].rearrange("p t e -> p (t e)")
                    pe.matmul(bank["m0"][:, 0:2 * E], tri[:, :], flat, start=True, stop=True)
                    pe.matmul(bank["m0"][:, 2 * E:4 * E], ones[:, :], flat, start=True, stop=True).then_inc(filled["m0"], 1)
                elif kind == "decays":
                    open_bank(g, "m0", "e")
                    pe.wait_ge(e_step, 3 * (g.n + 2))
                    for t in range(2):
                        mm = pe.transpose(bank["m0"][0:32, t * P:(t + 1) * P],
                                          e_hl[:, t, :, :].rearrange("p a h -> p (a h)").bitcast(F32), ident[:, :])
                    mm.then_inc(filled["m0"], 1)
                elif kind == "unit":
                    b = f"pj{c % 2}"
                    open_bank(g, b, f"u{c}")
                    for j in range(2):
                        col = slice((2 * c + j) * P, (2 * c + j + 1) * P)
                        mm = split3(bank[b][:, j * GT:(j + 1) * GT],
                                    [((wT_hi[:, k, col], wT_lo[:, k, col]), (xT_hi[:, k, :], xT_lo[:, k, :])) for k in range(KC)])
                    mm.then_inc(filled[b], 1)
                elif kind == "z":
                    b = f"pj{c}"
                    open_bank(g, b, f"z{c}")
                    tk = slice(c * P, (c + 1) * P)
                    split3(bank[b][:, :], [((xT_hi[:, k, tk], xT_lo[:, k, tk]), (wT_hi[:, k, C3:C3 + D], wT_lo[:, k, C3:C3 + D]))
                                           for k in range(KC)]).then_inc(filled[b], 1)
                elif kind == "oT":
                    open_bank(g, "m1", f"oT{c}")
                    pe.wait_ge(og_ready, g.chunk(c) + 1)
                    for k in range(KC):
                        mm = pe.transpose(bank["m1"][:, k * P:(k + 1) * P], og[:, k * P:(k + 1) * P], ident[:, :])
                    mm.then_inc(filled["m1"], 1)
                elif kind == "out":
                    open_bank(g, "m1", f"out{c}")
                    split3(bank["m1"][:, :], [((oT_hi[:, k, :], oT_lo[:, k, :]), (wT_hi[:, k, C3 + D:WCOLS], wT_lo[:, k, C3 + D:WCOLS]))
                                              for k in range(KC)]).then_inc(filled["m1"], 1)

        steps_of(pe, GROUPS, body)

    @block.scalar
    def _(act):
        for i in range(len(ROWS)):
            act.wait_ge(rows_turned, i + 1)
            act.copy(wT_hi[:, :, i * P:(i + 1) * P], bank[f"m{i % 2}"][:, :].rearrange("p (k c) -> p k c", k=KC)).then_inc(wT_hi_ready, 1)
        act.wait_ge(small_loaded, 64)
        act.activation(negA[:, :], negA[:, :], ACT.Exp).then_inc(negA_ready, 1)

        def body(g):
            cur, nxt = qkv[g.parity], 1 - g.parity
            for st in g.stages:
                kind, c = st[0], st[1]
                if kind == "stats":
                    act.wait_ge(mv_ready, 2 * (g.n + 2))
                    act.activation(ln_sd[:, :], mv[:, :, 1], ACT.Sqrt, bias=eps_ln[:, :]).then_inc(ln_sd_ready, 1)
                elif kind == "xn":
                    act.wait_ge(nmr_ready, g.n + 2)
                    after(act, xs_ready, 2 * (g.n + 1))
                    for t in range(2):
                        act.activation(xn[:, t, :], xin[nxt][:, t, :], ACT.Identity, bias=nmr[:, t:t + 1], scale=rstd[:, t:t + 1]).then_inc(xn_ready, 1)
                elif kind in ("squares", "next_squares"):
                    of = g.n + (kind == "next_squares")
                    act.wait_ge(qkv_ready, NU * of + 2)
                    act.activation(sq[:, :, :], qkv[nxt if kind == "next_squares" else g.parity][:, 0:QT, c * P:(c + 1) * P],
                                   ACT.Square).then_inc(sq_ready, 1)
                elif kind == "kT":
                    act.wait_ge(filled["m0"], g.fill("m0", f"kT{c}"))
                    act.copy(k_tm[:, :], bank["m0"][:, :]).then_inc(emptied["m0"], 1)
                    act.wait_ge(emptied["m0"], g.fill("m0", f"kT{c}"))
                    after(act, kss_ready, g.chunk(c))
                    act.activation(ksq[:, :], k_tm[:, :], ACT.Square).then_inc(ksq_ready, 1)
                elif kind == "norms":
                    act.wait_ge(filled["kv"], g.fill("kv", f"ss{c}"))
                    act.activation(nsd[:, 0:H], bank["kv"][:, 0:H], ACT.Sqrt, bias=eps_n[:, :]).then_inc(emptied["kv"], 1)
                    act.wait_ge(kss_ready, g.chunk(c) + 1)
                    act.activation(nsd[:, H:2 * H], kss[:, :], ACT.Sqrt, bias=eps_n[:, :]).then_inc(ksd_ready, 1)
                elif kind == "rms":
                    act.wait_ge(ovar_ready, g.chunk(c) + 1)
                    act.activation(osd[:, :], ovar[:, :], ACT.Sqrt, bias=eps_n[:, :], scale=1.0 / HD).then_inc(osd_ready, 1)
                elif kind == "xT":
                    for b, at in enumerate(XBANKS):
                        act.wait_ge(filled[at], g.fill(at, f"x{b}"))
                        act.copy(xT_hi[:, 2 * b:2 * b + 2, :], bank[at][:, :].rearrange("p (k t) -> p k t", k=2)).then_inc(xT_hi_ready, 1)
                elif kind == "gates":
                    act.wait_ge(route_step, ROUTE * (g.n + 1) + 7)
                    act.activation(lexp[:, :, :], lsub[:, :, :], ACT.Exp).then_inc(lexp_ready, 1)
                    act.activation(bexp[:, :, :], gl[:, :, BCOL], ACT.Exp, scale=-1.0).then_inc(bexp_ready, 1)
                    act.activation(yexp[:, :, :], aabs[:, :, :], ACT.Exp, scale=-1.0).then_inc(yexp_ready, 1)
                elif kind == "softplus":
                    act.wait_ge(soft_step, SOFT * (g.n + 2))
                    act.activation(e_raw[:, :, :], dec[:, :, :], ACT.Exp).then_inc(e_raw_ready, 1)
                elif kind == "decays":
                    act.wait_ge(filled["m0"], g.fill("m0", "e"))
                    act.copy(eT[nxt][:, :, :], bank["m0"][0:32, 0:2 * P].rearrange("p (t i) -> p t i", t=2)).then_inc(emptied["m0"], 1)
                elif kind == "pre":
                    b, U = f"pj{c % 2}", NU * (g.n + 1) + c
                    act.wait_ge(filled[b], g.fill(b, f"u{c}"))
                    after(act, conv_step, 6 * (U - 1))
                    after(act, halo_saved, U - 1)
                    act.copy(pre[c % 2][:, :, 3:3 + GT], bank[b][:, :].rearrange("p (j t) -> p j t", j=2)).then_inc(emptied[b], 1)
                    act.wait_ge(emptied[b], g.fill(b, f"u{c}"))
                    for j in range(2):
                        act.activation(qkv[nxt][:, 2 * c + j, :], pre[c % 2][:, j, 3:3 + GT], ACT.Copy, scale=cw[:, 2 * c + j, 3:4]).then_inc(tap_ready, 1)
                    if c in POOL_TAPS:
                        act.wait_ge(halo_in, U + 1)
                    for j in range(2 * (c in POOL_TAPS)):
                        act.activation(tap0[c % 2][:, j, :], pre[c % 2][:, j, 0:GT], ACT.Copy, scale=cw[:, 2 * c + j, 0:1]).then_inc(tap_ready, 1)
                elif kind == "silu_z":
                    b = f"pj{c}"
                    act.wait_ge(filled[b], g.fill(b, f"z{c}"))
                    after(act, oz_ready, 2 * g.n - 1 + c)
                    act.activation(sz[:, c, :], bank[b][:, :], ACT.Silu).then_inc(emptied[b], 1)
                elif kind in ("silu", "late_silu"):
                    late = kind == "late_silu"
                    act.wait_ge(conv_step, 6 * (NU * (g.n + (not late)) + c + 1))
                    v = qkv[g.parity if late else nxt][:, 2 * c:2 * c + 2, :]
                    act.activation(v, v, ACT.Silu).then_inc(qkv_ready, 1)
                elif kind == "finish":
                    q = g.chunk(c)
                    act.wait_ge(emptied["o"], g.fill("o", f"o{c}"))
                    after(act, ovar_ready, q)
                    act.activation(osq[:, :], o1[:, :], ACT.Square).then_inc(osq_ready, 1)
                elif kind == "oHi":
                    act.wait_ge(filled["m1"], g.fill("m1", f"oT{c}"))
                    act.copy(oT_hi[:, :, :], bank["m1"][:, :].rearrange("p (k t) -> p k t", k=KC)).then_inc(oT_hi_ready, 1)
                elif kind == "out":
                    q = g.chunk(c)
                    mine = nxt if c == "prev" else g.parity
                    after(act, ob_stored, 16 * q)
                    act.wait_ge(xs_ready, 2 * (g.n + (c != "prev")))
                    act.activation(fd[:, :], xs[mine][:, 1 if c == "prev" else c, :], ACT.Silu).then_inc(fd_ready, 1)
                    act.wait_ge(filled["m1"], g.fill("m1", f"out{c}"))
                    after(act, s_stored, 16 * q)
                    act.copy(s_sb[:, :], bank["m1"][:, :]).then_inc(emptied["m1"], 1)

        steps_of(act, GROUPS, body)

    @block.vector
    def _(dve):
        dve.memset(bias_row[:, BCOL], 0.0).then_inc(wg_step, 1)
        for i in range(len(ROWS)):
            dve.wait_ge(wT_hi_ready, i + 1)
            col = slice(i * P, (i + 1) * P)
            dve.tensor_tensor(wT_lo[:, :, col], bank[f"m{i % 2}"][:, :].rearrange("p (k c) -> p k c", k=KC),
                              wT_hi[:, :, col].bitcast(F32), ALU.subtract).then_inc(wT_lo_ready, 1)
        dve.wait_ge(gate_turned, 1)
        dve.tensor_copy(wg[:, :, E:NG], bank["eb"][:, 0:KC * 2 * H].rearrange("p (k h) -> p k h", k=KC)).then_inc(gate_turned, 1)
        dve.wait_ge(gate_turned, 2)
        dve.tensor_copy(wg_hl[:, :, 0, :], wg[:, :, :]).then_inc(wg_step, 1)
        dve.wait_ge(wg_step, 2)
        dve.tensor_tensor(wg_hl[:, :, 1, :], wg[:, :, :], wg_hl[:, :, 0, :].bitcast(F32), ALU.subtract).then_inc(wg_step, 1)
        dve.wait_ge(negA_ready, 1)
        dve.tensor_scalar(negA[:, :], negA[:, :], -1.0, None, ALU.mult).then_inc(negA_ready, 1)
        dve.wait_ge(negA_ready, 2)
        dve.wait_ge(const_ready, 1)

        def body(g):
            cur, nxt = qkv[g.parity], 1 - g.parity
            r0, f0, e0 = ROUTE * (g.n + 1), FACTOR * (g.n + 1), 3 * (g.n + 1)
            for st in g.stages:
                kind, c = st[0], st[1]
                q = g.chunk(c) if c == "prev" or kind not in NEXT else None
                if kind == "stats":
                    dve.wait_ge(x_loaded[nxt], 16 * (g.half + 1 + g.parity))
                    for t in range(2):
                        dve.bn_stats(bn[:, t, :], xin[nxt][:, t, :]).then_inc(bn_ready, 1)
                    dve.wait_ge(bn_ready, 2 * (g.n + 2))
                    dve.sem_inc(dve_held, 1)
                    for t in range(2):
                        dve.bn_aggr(mv[:, t, :], bn[:, t, :]).then_inc(mv_ready, 1)
                elif kind == "xn":
                    dve.wait_ge(ln_sd_ready, g.n + 2)
                    dve.reciprocal(rstd[:, :], ln_sd[:, :]).then_inc(rstd_ready, 1)
                    dve.wait_ge(rstd_ready, g.n + 2)
                    dve.scalar_tensor_tensor(nmr[:, :], mv[:, :, 0], -1.0, rstd[:, :], ALU.mult, ALU.mult).then_inc(nmr_ready, 1)
                elif kind == "norms":
                    dve.wait_ge(emptied["kv"], g.fill("kv", f"ss{c}"))
                    dve.wait_ge(ksd_ready, q + 1)
                    dve.reciprocal(rqk[:, :], nsd[:, :]).then_inc(rqk_ready, 1)
                    dve.wait_ge(rqk_ready, q + 1)
                    dve.tensor_tensor(vscale[:, :], rqk[:, H:2 * H], beta[g.parity][:, c, :], ALU.mult).then_inc(vscale_ready, 1)
                elif kind == "k_sum":
                    dve.wait_ge(ksq_ready, q + 1)
                    dve.tensor_reduce(kss[:, :], heads(ksq[:, :]), AX.X, ALU.add).then_inc(kss_ready, 1)
                elif kind == "vp":
                    dve.wait_ge(filled["m1"], g.fill("m1", f"vT{c}"))
                    dve.wait_ge(vscale_ready, q + 1)
                    after(dve, vw_ready, q)
                    dve.tensor_tensor(heads(vp[:, :]), heads(bank["m1"][:, :]), vscale[:, :].unsqueeze(2).to_broadcast([P, H, HD]),
                                      ALU.mult).then_inc(emptied["m1"], 1)
                elif kind == "decay_cm":
                    dve.wait_ge(filled["eb"], g.fill("eb", f"cd{c}"))
                    for t in range(QT):
                        op = dve.tensor_tensor_scan(cdT[:, t, :], bank["eb"][:, t * P:(t + 1) * P], zeros[:, :], 1.0, ALU.mult, ALU.add)
                    op.then_inc(emptied["eb"], 1)
                    dve.wait_ge(emptied["eb"], g.fill("eb", f"cd{c}"))
                    dve.tensor_tensor(qd[:, :, :], cur[:, 0:QT, c * P:(c + 1) * P], cdT[:, :, :], ALU.mult).then_inc(qd_ready, 1)
                    after(dve, state_ready, q)
                    dve.tensor_copy(cdlast[c][:, :], cdT[:, :, P - 1]).then_inc(cdlast_ready, 1)
                elif kind == "tile":
                    t = st[2]
                    dve.wait_ge(filled["eb"], g.fill("eb", f"e{st[1:]}"))
                    after(dve, wlast_ready, 4 * q + t - 1)
                    dve.tensor_tensor_scan(dm[t % 2][:, :], bank["eb"][:, :], ident4[:, :], 0.0, ALU.mult, ALU.add).then_inc(emptied["eb"], 1)
                    dve.wait_ge(emptied["eb"], g.fill("eb", f"e{st[1:]}"))
                    dve.wait_ge(filled["sc"], g.fill("sc", f"s{st[1:]}"))
                    after(dve, weighed, 4 * q + t - 1)
                    dve.tensor_tensor(pm[t % 2][:, :], bank["sc"][:, :], dm[t % 2][:, :], ALU.mult).then_inc(emptied["sc"], 1)
                elif kind == "finish":
                    dve.wait_ge(filled["o"], g.fill("o", f"o{c}"))
                    after(dve, og_ready, q)
                    dve.scalar_tensor_tensor(heads(o1[:, :]), heads(bank["o"][:, :]), HD ** -0.5,
                                             rqk[:, 0:H].unsqueeze(2).to_broadcast([P, H, HD]), ALU.mult, ALU.mult).then_inc(emptied["o"], 1)
                    dve.wait_ge(filled["kv"], g.fill("kv", f"kv{c}"))
                    dve.wait_ge(state_ready, q + 1)
                    dve.tensor_tensor(kvm[:, :, :], bank["kv"][:, :].rearrange("p (t v) -> p t v", t=QT),
                                      bdmask[:, :].unsqueeze(1).to_broadcast([P, QT, P]), ALU.mult).then_inc(emptied["kv"], 1)
                elif kind == "rms":
                    dve.wait_ge(osq_ready, q + 1)
                    dve.tensor_reduce(ovar[:, :], heads(osq[:, :]), AX.X, ALU.add).then_inc(ovar_ready, 1)
                elif kind == "og":
                    dve.wait_ge(osd_ready, q + 1)
                    dve.reciprocal(orn[:, :], osd[:, :]).then_inc(orn_ready, 1)
                    dve.wait_ge(orn_ready, q + 1)
                    dve.wait_ge(oz_ready, q + 1)
                    dve.tensor_tensor(heads(og[:, :]), heads(oz[:, :]), orn[:, :].unsqueeze(2).to_broadcast([P, H, HD]), ALU.mult).then_inc(og_ready, 1)
                elif kind == "oLo":
                    dve.wait_ge(oT_hi_ready, q + 1)
                    dve.tensor_tensor(oT_lo[:, :, :], bank["m1"][:, :].rearrange("p (k t) -> p k t", k=KC),
                                      oT_hi[:, :, :].bitcast(F32), ALU.subtract).then_inc(emptied["m1"], 1)
                elif kind == "xT":
                    for b, at in enumerate(XBANKS):
                        dve.wait_ge(xT_hi_ready, 2 * (g.n + 1) + b + 1)
                        dve.tensor_tensor(xT_lo[:, 2 * b:2 * b + 2, :], bank[at][:, :].rearrange("p (k t) -> p k t", k=2),
                                          xT_hi[:, 2 * b:2 * b + 2, :].bitcast(F32), ALU.subtract).then_inc(emptied[at], 1)
                elif kind == "gates":
                    dve.wait_ge(filled["m0"], g.fill("m0", "g"))
                    part = bank["m0"][:, 0:4 * NG].rearrange("p (t a c) -> p t a c", t=2, a=2)
                    dve.tensor_tensor(gl[:, :, :], part[:, :, 0, :], bias_row[:, :].unsqueeze(1).to_broadcast([P, 2, NG]), ALU.add).then_inc(gl_ready, 1)
                    dve.wait_ge(gl_ready, g.n + 2)
                    dve.tensor_tensor(gl[:, :, :], gl[:, :, :], part[:, :, 1, :], ALU.add).then_inc(emptied["m0"], 1)
                    dve.wait_ge(emptied["m0"], g.fill("m0", "g"))
                    dve.tensor_reduce(mx[:, :], gl[:, :, LOGITS], AX.X, ALU.max).then_inc(route_step, 1)
                    dve.wait_ge(route_step, r0 + 1)
                    mxb = mx[:, :].unsqueeze(2).to_broadcast([P, 2, E])
                    dve.tensor_tensor(lsub[:, :, :], gl[:, :, LOGITS], mxb, ALU.subtract).then_inc(route_step, 1)
                    dve.tensor_tensor(eq[:, :, :], gl[:, :, LOGITS], mxb, ALU.is_equal).then_inc(route_step, 1)
                    dve.wait_ge(route_step, r0 + 3)
                    eb = eidx[:, :].unsqueeze(1).to_broadcast([P, 2, E])
                    dve.tensor_tensor(cand[:, :, :], eq[:, :, :], eb, ALU.mult).then_inc(route_step, 1)
                    dve.wait_ge(route_step, r0 + 4)
                    dve.tensor_reduce(rid[:, :], cand[:, :, :], AX.X, ALU.min).then_inc(route_step, 1)
                    dve.wait_ge(route_step, r0 + 5)
                    dve.tensor_tensor(oh[:, :, :], eb, rid[:, :].unsqueeze(2).to_broadcast([P, 2, E]), ALU.is_equal).then_inc(route_step, 1)
                    dve.scalar_tensor_tensor(aabs[:, :, :], gl[:, :, ACOL], -1.0, gl[:, :, ACOL], ALU.mult, ALU.max).then_inc(route_step, 1)
                elif kind == "route":
                    m0 = bank["m0"]
                    dve.wait_ge(filled["m0"], g.fill("m0", "r"))
                    dve.tensor_tensor(rank[:, :, :], m0[:, 0:2 * E].rearrange("p (t e) -> p t e", t=2),
                                      count[:, :].unsqueeze(1).to_broadcast([P, 2, E]), ALU.add).then_inc(route_step, 1)
                    dve.wait_ge(route_step, r0 + 8)
                    dve.tensor_tensor(rank[:, 1, :], rank[:, 1, :], m0[:, 2 * E:3 * E], ALU.add).then_inc(route_step, 1)
                    dve.tensor_tensor(count[:, :], count[:, :], m0[:, 2 * E:3 * E], ALU.add).then_inc(route_step, 1)
                    dve.wait_ge(route_step, r0 + 10)
                    dve.tensor_tensor(count[:, :], count[:, :], m0[:, 3 * E:4 * E], ALU.add).then_inc(emptied["m0"], 1)
                    dve.tensor_tensor(rank[:, :, :], rank[:, :, :], oh[:, :, :], ALU.mult).then_inc(route_step, 1)
                    dve.wait_ge(route_step, r0 + 11)
                    dve.wait_ge(emptied["m0"], g.fill("m0", "r"))
                    dve.tensor_reduce(pos[:, :], rank[:, :, :], AX.X, ALU.add).then_inc(route_step, 1)
                    dve.wait_ge(route_step, r0 + 12)
                    dve.tensor_scalar(over[:, :], pos[:, :], float(CAP), float(2 * NTOK), ALU.is_gt, ALU.mult).then_inc(route_step, 1)
                    dve.scalar_tensor_tensor(slot_f[:, :], rid[:, :], float(CAP), pos[:, :], ALU.mult, ALU.add).then_inc(factor_step, 1)
                    dve.wait_ge(route_step, r0 + 13)
                    dve.wait_ge(factor_step, f0 + 1)
                    after(dve, tok_scattered[nxt], 32 * (g.half + g.parity))
                    dve.scalar_tensor_tensor(slot[nxt][:, :], slot_f[:, :], float(E * CAP - 1), over[:, :], ALU.add, ALU.add).then_inc(slot_ready, 1)
                elif kind == "factor":
                    dve.wait_ge(lexp_ready, g.n + 2)
                    dve.tensor_reduce(lsum[:, :], lexp[:, :, :], AX.X, ALU.add).then_inc(factor_step, 1)
                    dve.wait_ge(factor_step, f0 + 2)
                    dve.reciprocal(pmax[:, :], lsum[:, :]).then_inc(factor_step, 1)
                    dve.wait_ge(factor_step, f0 + 3)
                    dve.reciprocal(rpmax[:, :], pmax[:, :]).then_inc(factor_step, 1)
                    dve.wait_ge(factor_step, f0 + 4)
                    dve.tensor_tensor(factor[:, :], pmax[:, :], rpmax[:, :], ALU.mult).then_inc(factor_step, 1)
                elif kind == "softplus":
                    k = SOFT * (g.n + 1)

                    def settled(steps):
                        dve.wait_ge(soft_step, k + steps)

                    dve.wait_ge(bexp_ready, g.n + 2)
                    dve.tensor_scalar(bexp[:, :, :], bexp[:, :, :], 1.0, None, ALU.add).then_inc(soft_step, 1)
                    settled(1)
                    dve.reciprocal(beta[nxt][:, :, :], bexp[:, :, :]).then_inc(soft_step, 1)
                    dve.wait_ge(yexp_ready, g.n + 2)
                    dve.tensor_scalar(yden[:, :, :], yexp[:, :, :], 2.0, None, ALU.add).then_inc(soft_step, 1)
                    settled(3)
                    dve.reciprocal(yden[:, :, :], yden[:, :, :]).then_inc(soft_step, 1)
                    settled(4)
                    dve.scalar_tensor_tensor(sat[:, :, :], yexp[:, :, :], 2.0, yden[:, :, :], ALU.mult, ALU.mult).then_inc(soft_step, 1)
                    settled(5)
                    dve.tensor_tensor(sat2[:, :, :], sat[:, :, :], sat[:, :, :], ALU.mult).then_inc(soft_step, 1)
                    settled(6)
                    dve.tensor_scalar(poly[:, :, :], sat2[:, :, :], POLY[-1], None, ALU.mult).then_inc(soft_step, 1)
                    for j, coef in enumerate(reversed(POLY[:-1])):
                        settled(7 + j)
                        dve.scalar_tensor_tensor(poly[:, :, :], poly[:, :, :], coef, sat2[:, :, :], ALU.add, ALU.mult).then_inc(soft_step, 1)
                    n = 6 + len(POLY)
                    settled(n)
                    dve.scalar_tensor_tensor(poly[:, :, :], poly[:, :, :], 1.0, sat[:, :, :], ALU.add, ALU.mult).then_inc(soft_step, 1)
                    settled(n + 1)
                    dve.scalar_tensor_tensor(dec[:, :, :], gl[:, :, ACOL], 0.0, poly[:, :, :], ALU.max, ALU.add).then_inc(soft_step, 1)
                    settled(n + 2)
                    dve.tensor_tensor(dec[:, :, :], dec[:, :, :], negA[:, :].unsqueeze(1).to_broadcast([P, 2, H]), ALU.mult).then_inc(soft_step, 1)
                elif kind == "e_split":
                    dve.wait_ge(e_raw_ready, g.n + 2)
                    dve.tensor_scalar(e_raw[:, 0, :], e_raw[:, 0, :], column(keep_first, g.n + 1), None, ALU.mult).then_inc(e_step, 1)
                    dve.wait_ge(e_step, e0 + 1)
                    dve.tensor_copy(e_hl[:, :, 0, :], e_raw[:, :, :]).then_inc(e_step, 1)
                    dve.wait_ge(e_step, e0 + 2)
                    dve.tensor_tensor(e_hl[:, :, 1, :], e_raw[:, :, :], e_hl[:, :, 0, :].bitcast(F32), ALU.subtract).then_inc(e_step, 1)
                elif kind in ("conv", "late_conv"):
                    late = kind == "late_conv"
                    U = NU * (g.n + (not late)) + c
                    of = g.n + (not late)
                    if c in POOL_TAPS:
                        dve.wait_ge(first_tap_ready, first_taps(of, c))
                    else:
                        dve.wait_ge(halo_in, U + 1)
                        dve.wait_ge(tap_ready, taps(of, c))
                    mine = (1, 2) if c in POOL_TAPS else (0, 1, 2)
                    for k in mine:
                        if k != mine[0]:
                            dve.wait_ge(conv_step, 6 * U + 2 * k)
                        for j in range(2):
                            y = qkv[g.parity if late else nxt][:, 2 * c + j, :]
                            dve.scalar_tensor_tensor(y, pre[c % 2][:, j, k:k + GT], cw[:, 2 * c + j, k:k + 1], y, ALU.mult, ALU.add).then_inc(conv_step, 2 if k == 1 == mine[0] else 1)

        steps_of(dve, GROUPS, body)

    @block.gpsimd
    def _(pool):
        made = [0]

        def settle(op):
            made[0] += 1
            op.then_inc(const_made, 1)
            pool.wait_ge(const_made, made[0])

        def select(tile, pattern, op, fill, base=0, mult=1):
            settle(pool.affine_select(out=tile, in_=tile, pattern=pattern, compare_op=op, fill=fill, base=base, channel_multiplier=mult))

        settle(pool.memset(ident[:, :], 0.0))
        select(ident[:, :], [[-1, P]], ALU.not_equal, 1.0)
        settle(pool.tensor_copy(ident4[:, :].rearrange("p (h i) -> p h i", h=HPT), ident[:, :].unsqueeze(1).to_broadcast([P, HPT, P])))
        settle(pool.memset(ones[:, :], 1.0))
        settle(pool.memset(tri[:, :], 1.0))
        select(tri[:, :], [[1, P]], ALU.is_ge, 0.0, mult=-1)
        settle(pool.memset(headsum[:, :], 1.0))
        select(headsum[:, :], [[-HD, HPT]], ALU.is_ge, 0.0)
        select(headsum[:, :], [[HD, HPT]], ALU.is_ge, 0.0, base=HD - 1, mult=-1)
        settle(pool.tensor_copy(bdmask[:, :].rearrange("p (h v) -> p h v", h=HPT), headsum[:, :].unsqueeze(2).to_broadcast([P, HPT, HD])))
        settle(pool.memset(ind[:, :], 0.0))
        select(ind[:, :], [[-1, H]], ALU.not_equal, 1.0)
        select(ind[:, :], [[-1, H]], ALU.not_equal, 1.0, base=-H)
        settle(pool.tensor_copy(ind_r[:, :], ind[:, :]))
        settle(pool.tensor_copy(ind_cm[:, :].rearrange("p (h d) -> p h d", d=HD), ind[:, :].unsqueeze(2).to_broadcast([32, H, HD])))
        settle(pool.memset(zeros[:, :], 0.0))
        settle(pool.memset(keep_first[:, :], 1.0))
        settle(pool.memset(keep_first[0:1, 0:GROUPS:PER_BATCH], 0.0))
        settle(pool.memset(keep_halo[:, :], 1.0))
        settle(pool.memset(keep_halo[:, 0:GROUPS:PER_BATCH], 0.0))
        settle(pool.iota(eidx[:, :], [[1, E]], base=-E, channel_multiplier=0, allow_small_or_imprecise_dtypes=True))
        settle(pool.iota(tok_f[:, :], [[P, 2]], base=0, channel_multiplier=1, allow_small_or_imprecise_dtypes=True))
        settle(pool.memset(eps_ln[:, :], 1e-5))
        settle(pool.memset(eps_n[:, :], 1e-6))
        settle(pool.memset(no_token[:, :], NO_TOKEN))
        settle(pool.memset(halo[:, :, :], 0.0))
        settle(pool.memset(count[:, :], 0.0))
        settle(pool.memset(state[:, :, :], 0.0))
        pool.sem_inc(const_ready, 1)
        pool.sem_inc(state_ready, 1)
        pool.wait_ge(tok_cleared, 16)

        def body(g):
            cur, nxt = qkv[g.parity], 1 - g.parity
            for st in g.stages:
                kind, c = st[0], st[1]
                q = g.chunk(c) if c == "prev" or kind not in NEXT else None
                if kind in ("qblocks", "next_qblocks"):
                    ahead = kind == "next_qblocks"
                    cur = qkv[nxt if ahead else g.parity]
                    pool.wait_ge(qkv_ready, NU * (g.n + ahead) + 2)
                    if g.stages is not FRONT:
                        pool.wait_ge(filled["sc"], g.fill("sc", f"s{(1 - c, 3)}"))
                    pool.sem_inc(pool_held, 1)
                    for h in range(HPT):
                        pool.tensor_scalar(qbd[:, :, h, :], cur[:, 0:QT, c * P:(c + 1) * P], headsum[:, h:h + 1], 1.0,
                                           ALU.mult, ALU.mult).then_inc(qbd_ready, 1)
                elif kind == "tile":
                    t = st[2]
                    pool.wait_ge(emptied["eb"], g.fill("eb", f"e{st[1:]}"))
                    pool.sem_inc(pool_held, 1)
                    pool.tensor_copy(wlast[:, t * HPT:(t + 1) * HPT], dm[t % 2][:, P - 1:HPT * P:P]).then_inc(wlast_ready, 1)
                elif kind == "vw":
                    pool.wait_ge(wlast_ready, 4 * (q + 1))
                    pool.wait_ge(emptied["m1"], g.fill("m1", f"vT{c}"))
                    pool.tensor_tensor(heads(vw[:, :]), heads(vp[:, :]), wlast[:, :].unsqueeze(2).to_broadcast([P, H, HD]), ALU.mult).then_inc(vw_ready, 1)
                elif kind == "finish":
                    pool.wait_ge(filled["o"], g.fill("o", f"o{c}"))
                    pool.wait_ge(cdlast_ready, q + 1)
                    pool.tensor_tensor(state[:, :, :], state[:, :, :], cdlast[c][:, :].unsqueeze(2).to_broadcast([P, QT, P]), ALU.mult).then_inc(state_decayed, 1)
                    pool.wait_ge(state_decayed, q + 1)
                    pool.wait_ge(emptied["kv"], g.fill("kv", f"kv{c}"))
                    pool.tensor_tensor(state[:, :, :], state[:, :, :], kvm[:, :, :], ALU.add).then_inc(state_ready, 1)
                    pool.wait_ge(emptied["o"], g.fill("o", f"o{c}"))
                    pool.wait_ge(emptied[f"pj{c}"], g.fill(f"pj{c}", f"z{c}"))
                    pool.wait_ge(osq_ready, q + 1)
                    pool.tensor_tensor(oz[:, :], o1[:, :], sz[:, c, :], ALU.mult).then_inc(oz_ready, 1)
                elif kind == "out":
                    pool.wait_ge(fd_ready, q + 1)
                    pool.wait_ge(emptied["m1"], g.fill("m1", f"out{c}"))
                    pool.tensor_tensor(ob[:, :], s_sb[:, :], fd[:, :], ALU.mult).then_inc(ob_step, 1)
                    pool.wait_ge(ob_step, q + 1)
                    pool.wait_ge(xr_loaded, 16 * (q + 1))
                    pool.tensor_tensor(ob[:, :], ob[:, :], xr[:, :], ALU.add).then_inc(ob_ready, 1)
                elif kind == "factor":
                    pool.wait_ge(factor_step, FACTOR * (g.n + 2))
                    pool.wait_ge(xn_ready, 2 * (g.n + 2))
                    after(pool, fd_ready, 2 * g.n)
                    after(pool, xs_stored[nxt], 16 * (g.half + g.parity))
                    pool.sem_inc(pool_held, 1)
                    for t in range(2):
                        pool.tensor_scalar(xs[nxt][:, t, :], xn[:, t, :], factor[:, t:t + 1], 1.0, ALU.mult, ALU.mult).then_inc(xs_ready, 1)
                    after(pool, tok_scattered[nxt], 32 * (g.half + g.parity))
                    pool.sem_inc(pool_held, 1)
                    pool.tensor_copy(tok[nxt][:, :], tok_f[:, :]).then_inc(tok_step, 1)
                    pool.wait_ge(tok_step, 2 * (g.n + 1) + 1)
                    pool.sem_inc(pool_held, 1)
                    pool.tensor_scalar(tok_f[:, :], tok_f[:, :], float(GT), 1.0, ALU.add, ALU.mult).then_inc(tok_step, 1)
                    pool.wait_ge(tok_step, 2 * (g.n + 2))
                    pool.wait_ge(slot_ready, g.n + 2)
                    pool.sem_inc(pool_held, 1)
                    for t in range(2):
                        pool.indirect_dma_start(
                            out=tok_tab, out_offset=bass.IndirectOffsetOnAxis(ap=slot[nxt][:, t:t + 1].bitcast(U32), axis=0),
                            in_=tok[nxt][:, t:t + 1], in_offset=None, bounds_check=NTOK - 1, oob_is_err=False).then_inc(tok_scattered[nxt], 16)
                elif kind == "turned_decays":
                    pool.wait_ge(emptied["m0"], g.fill("m0", "e"))
                    pool.sem_inc(pool_held, 1)
                    pool.tensor_copy(eTz[nxt][:, :, :], eT[nxt][:, :, :].bitcast(F32)).then_inc(eTz_step, 1)
                    pool.wait_ge(eTz_step, 2 * (g.n + 1) + 1)
                    pool.sem_inc(pool_held, 1)
                    pool.tensor_copy(eTz[nxt][:, :, 0], zeros[0:32, 0:2]).then_inc(eTz_step, 1)
                elif kind == "pre":
                    U = NU * (g.n + 1) + c
                    cols = slice(2 * c, 2 * c + 2)
                    after(pool, conv_step, 6 * (U - 1))
                    after(pool, halo_saved, U)
                    pool.sem_inc(pool_held, 1)
                    pool.tensor_tensor(pre[c % 2][:, :, 0:3], halo[:, cols, :],
                                       column(keep_halo, g.n + 1).unsqueeze(2).to_broadcast([P, 2, 3]), ALU.mult).then_inc(halo_in, 1)
                    pool.wait_ge(halo_in, U + 1)
                    b = f"pj{c % 2}"
                    pool.wait_ge(emptied[b], g.fill(b, f"u{c}"))
                    pool.sem_inc(pool_held, 1)
                    pool.tensor_copy(halo[:, cols, :], pre[c % 2][:, :, GT:GT + 3]).then_inc(halo_saved, 1)
                    if c in POOL_TAPS:
                        pool.wait_ge(tap_ready, taps(g.n + 1, c))
                        y = qkv[nxt][:, cols, :]
                        pool.tensor_tensor(y, y, tap0[c % 2][:, :, :], ALU.add).then_inc(first_tap_ready, 1)

        steps_of(pool, GROUPS, body)
        for i in range(2):
            pool.wait_ge(tok_scattered[i], 32 * (GROUPS // 2))


def phase_b(nc, ctx, bank, ident, xf, outf, xs_tab, s_tab, tok_tab, W1, b1, W2, b2):
    NTOK, D = xf.shape
    E, _, FF = W1.shape
    KC = D // P
    CAP = NTOK // E
    FT = FF // P
    HS = 512
    PASSES = CAP // HS
    ST = HS // P
    CH = 4
    NCH = FT // CH
    NYB = 4
    TURN = FT // 2
    assert PASSES == 2 and ST == NYB

    def sb(name, shape, dt=F32):
        return ctx.enter_context(nc.sbuf_tensor(name, shape, dt))

    def sem(name):
        return ctx.enter_context(nc.semaphore(name))

    w1_raw = sb("w1_raw", [P, KC, FF])
    w2_raw = sb("w2_raw", [P, FT, D])
    w1_hi = [sb(f"w1_hi{i}", [P, KC, P], F32R) for i in range(2)]
    w1_lo = [sb(f"w1_lo{i}", [P, KC, P], F32R) for i in range(2)]
    w2_hi = [sb(f"w2_hi{i}", [P, D], F32R) for i in range(2)]
    w2_lo = [sb(f"w2_lo{i}", [P, D], F32R) for i in range(2)]
    xT_hi = [sb(f"bxT_hi{i}", [P, KC, HS], F32R) for i in range(2)]
    xT_lo = [sb(f"bxT_lo{i}", [P, KC, HS], F32R) for i in range(2)]
    hid = [sb(f"hid{i}", [P, HS]) for i in range(2)]
    hid_hi = [sb(f"hid_hi{i}", [P, HS], F32R) for i in range(2)]
    hid_lo = [sb(f"hid_lo{i}", [P, HS], F32R) for i in range(2)]
    xg = sb("xg", [P, ST, D])
    x_rows = sb("x_rows", [P, ST, D])
    s_rows = sb("s_rows", [P, ST, D])
    y = sb("y", [P, ST, D])
    tok = [sb(f"btok{i}", [P, ST], I32) for i in range(2)]
    b1_rows = sb("b1_rows", [P, P])
    b1_cols = sb("b1_cols", [P, E, FT])
    b1_e = sb("b1_e", [P, FT])
    b2_row = sb("b2_row", [P, D])

    ybank = [bank[b] for b in ("pj0", "pj1", "eb", "sc")]
    hbank = [bank["o"], bank["kv"]]
    tbank = [bank["m0"], bank["m1"]]
    raw_loaded = [sem(f"raw_loaded{i}") for i in range(2)]
    (tok_loaded, rows_cleared, xs_gathered, rows_gathered, b1_loaded, b1_turned, b1_ready, b1e_ready, b2_loaded,
     t_filled, bxT_hi_ready, t_emptied, w1_hi_ready, w1_lo_ready, w2_hi_ready, w2_lo_ready, h_filled, hid_ready,
     hid_hi_ready, hid_lo_ready, y_filled, y_added, y_emptied, y_gated, y_scaled, y_done, y_scattered) = (
         sem(n) for n in (
             "tok_loaded rows_cleared xs_gathered rows_gathered b1_loaded b1_turned b1_ready b1e_ready b2_loaded "
             "t_filled bxT_hi_ready t_emptied w1_hi_ready w1_lo_ready w2_hi_ready w2_lo_ready h_filled hid_ready "
             "hid_hi_ready hid_lo_ready y_filled y_added y_emptied y_gated y_scaled y_done y_scattered").split())

    tok_u = tok_tab.rearrange("(u p s) o -> u p (s o)", p=P, s=ST)
    w1_e = W1.rearrange("e (k p) f -> e p k f", p=P)
    w2_e = W2.rearrange("e (f p) d -> e p f d", p=P)
    b2_e = b2.rearrange("e (a d) -> e a d", a=1)

    def experts(eng, body):
        body(0, False)
        with eng.Fori(1, E - 1) as e:
            body(e, False)
        body(E - 1, True)

    pool_held, sp_held, dve_held = sem("pool_held"), sem("sp_held"), sem("dve_held")
    block = ctx.enter_context(nc.Block())


    @block.sync
    def _(sp):
        sp.dma_start(b1_rows[:, :], b1.rearrange("e (f p) -> (e f) p", p=P)).then_inc(b1_loaded, 16)
        sp.dma_start(tok[0][:, :], tok_u[0]).then_inc(tok_loaded, 16)

        def load(e, first):
            for c in range(NCH):
                fs, fd = slice(c * CH * P, (c + 1) * CH * P), slice(c * CH, (c + 1) * CH)
                if not first:
                    k = FT * (PASSES * e - 1) + CH * (c + 1)
                    sp.wait_ge(w1_lo_ready, k)
                    sp.sem_inc(sp_held, 1)
                    sp.wait_ge(w2_lo_ready, k)
                    sp.sem_inc(sp_held, 1)
                after(sp, raw_loaded[c % 2], 32 * (NCH // 2 * e + c // 2))
                sp.sem_inc(sp_held, 1)
                sp.dma_start(w1_raw[:, :, fs], row(w1_e, e)[:, :, fs]).then_inc(raw_loaded[c % 2], 16)
                sp.sem_inc(sp_held, 1)
                sp.dma_start(w2_raw[:, fd, :], row(w2_e, e)[:, fd, :]).then_inc(raw_loaded[c % 2], 16)
            if not first:
                sp.wait_ge(y_emptied, ST * PASSES * e)
            sp.sem_inc(sp_held, 1)
            sp.dma_start(b2_row[:, :], row(b2_e, e).partition_broadcast(P)).then_inc(b2_loaded, 16)

        load(0, True)

        def body(e, last):
            for a in range(PASSES):
                u = PASSES * e + a
                if not (last and a == PASSES - 1):
                    after(sp, y_scattered, 16 * ST * u)
                    sp.sem_inc(sp_held, 1)
                    sp.dma_start(tok[1 - a][:, :], row(tok_u, u + 1)).then_inc(tok_loaded, 16)
            if not last:
                load(e + 1, False)

        experts(sp, body)

    @block.gpsimd
    def _(pool):
        pool.memset(xg[:, :, :], 0.0).then_inc(rows_cleared, 1)
        pool.wait_ge(rows_cleared, 1)

        def gather(dst, table, numbers, done):
            pool.sem_inc(pool_held, 1)
            for t in range(ST):
                pool.indirect_dma_start(out=dst[:, t, :], out_offset=None, in_=table,
                                        in_offset=bass.IndirectOffsetOnAxis(ap=numbers[:, t:t + 1].bitcast(U32), axis=0),
                                        bounds_check=NTOK - 1, oob_is_err=False).then_inc(done, 16)

        pool.wait_ge(tok_loaded, 16)
        gather(xg, xs_tab, tok[0], xs_gathered)
        pool.memset(x_rows[:, :, :], 0.0).then_inc(rows_cleared, 1)
        pool.memset(s_rows[:, :, :], 0.0).then_inc(rows_cleared, 1)
        pool.wait_ge(rows_cleared, 3)

        def body(e, last):
            for a in range(PASSES):
                u = PASSES * e + a
                if not (last and a == PASSES - 1):
                    pool.wait_ge(tok_loaded, 16 * (u + 2))
                    pool.wait_ge(t_filled, KC * (u + 1))
                    gather(xg, xs_tab, tok[1 - a], xs_gathered)
                gather(x_rows, xf, tok[a], rows_gathered)
                gather(s_rows, s_tab, tok[a], rows_gathered)
                pool.sem_inc(pool_held, 1)
                for t in range(ST):
                    i = ST * u + t
                    if t == 0:
                        pool.wait_ge(rows_gathered, 16 * 2 * ST * (u + 1))
                    pool.wait_ge(y_gated, i + 1)
                    pool.tensor_tensor(s_rows[:, t, :], s_rows[:, t, :], y[:, t, :], ALU.mult).then_inc(y_scaled, 1)
                    pool.wait_ge(y_scaled, i + 1)
                    pool.tensor_tensor(x_rows[:, t, :], x_rows[:, t, :], s_rows[:, t, :], ALU.add).then_inc(y_done, 1)
                    pool.wait_ge(y_done, i + 1)
                    pool.sem_inc(pool_held, 1)
                    pool.indirect_dma_start(out=outf, out_offset=bass.IndirectOffsetOnAxis(ap=tok[a][:, t:t + 1].bitcast(U32), axis=0),
                                            in_=x_rows[:, t, :], in_offset=None, bounds_check=NTOK - 1, oob_is_err=False).then_inc(y_scattered, 16)
                pool.wait_ge(y_scattered, 16 * ST * (u + 1))

        experts(pool, body)

    @block.tensor
    def _(pe):
        pe.wait_ge(b1_loaded, 16)
        pe.transpose(tbank[0][:, 0:P], b1_rows[:, :], ident[:, :]).then_inc(b1_turned, 1)
        pe.wait_ge(b1_ready, 1)

        def turn(u, k):
            if k == 0:
                pe.wait_ge(xs_gathered, 16 * ST * (u + 1))
            after(pe, t_emptied, KC * u + k - 1)
            for t in range(ST):
                mm = pe.transpose(tbank[k % 2][:, t * P:(t + 1) * P], xg[:, t, k * P:(k + 1) * P], ident[:, :])
            mm.then_inc(t_filled, 1)

        def layer1(u, a, f):
            k, i = FT * u + f, f % 2
            pe.wait_ge(w1_lo_ready, k + 1)
            if f == 0:
                pe.wait_ge(t_emptied, KC * (u + 1))
            after(pe, hid_ready, k - 1)
            n = 0
            for c in range(KC):
                for w, xt in ((w1_hi, xT_hi), (w1_hi, xT_lo), (w1_lo, xT_hi)):
                    mm = pe.matmul(hbank[i][:, :], w[i][:, c, :], xt[a][:, c, :], start=(n == 0), stop=(n == 3 * KC - 1))
                    n += 1
            mm.then_inc(h_filled, 1)

        def layer2(u, f):
            k, i = FT * u + f, f % 2
            pe.wait_ge(w2_lo_ready, k + 1)
            pe.wait_ge(hid_lo_ready, k + 1)
            for t in range(ST):
                if f == 0:
                    after(pe, y_emptied, ST * (u - 1) + t + 1)
                tk = slice(t * P, (t + 1) * P)
                for n, (h, w) in enumerate(((hid_hi, w2_hi), (hid_hi, w2_lo), (hid_lo, w2_hi))):
                    mm = pe.matmul(ybank[t][:, :], h[i][:, tk], w[i][:, :], start=(f == 0 and n == 0), stop=(f == FT - 1 and n == 2))
            mm.then_inc(y_filled, 1)

        for k in range(KC):
            turn(0, k)
        layer1(0, 0, 0)

        def body(e, last):
            for a in range(PASSES):
                u = PASSES * e + a
                final = last and a == PASSES - 1
                for f in range(FT):
                    if TURN <= f < TURN + KC and not final:
                        turn(u + 1, f - TURN)
                    if f < FT - 1:
                        layer1(u, a, f + 1)
                    elif not final:
                        layer1(u + 1, 1 - a, 0)
                    layer2(u, f)

        experts(pe, body)

    @block.scalar
    def _(act):
        def turned(u, a, k):
            act.wait_ge(t_filled, KC * u + k + 1)
            act.copy(xT_hi[a][:, k, :], tbank[k % 2][:, :]).then_inc(bxT_hi_ready, 1)

        def split_w1(e, a, f):
            if a == 0 and f % CH == 0:
                act.wait_ge(raw_loaded[f // CH % 2], 32 * (NCH // 2 * e + f // CH // 2 + 1))
            act.copy(w1_hi[f % 2][:, :, :], w1_raw[:, :, f * P:(f + 1) * P]).then_inc(w1_hi_ready, 1)

        def split_w2(k, f):
            after(act, y_filled, k - 1)
            act.copy(w2_hi[f % 2][:, :], w2_raw[:, f, :]).then_inc(w2_hi_ready, 1)

        def gate(u, tiles):
            for t in tiles:
                act.wait_ge(y_emptied, ST * u + t + 1)
                act.activation(y[:, t, :], y[:, t, :], ACT.Silu).then_inc(y_gated, 1)

        def body(e, last):
            for a in range(PASSES):
                u = PASSES * e + a
                final = last and a == PASSES - 1
                for f in range(FT):
                    k, i = FT * u + f, f % 2
                    if TURN <= f - 1 < TURN + KC and not final:
                        turned(u + 1, 1 - a, f - 1 - TURN)
                    act.wait_ge(h_filled, k + 1)
                    if a == 0 and f in (0, FT // 2):
                        act.wait_ge(b1e_ready, 2 * e + 1 + f // (FT // 2))
                    act.activation(hid[i][:, :], hbank[i][:, :], ACT.Gelu, bias=b1_e[:, f:f + 1], scale=GELU_R).then_inc(hid_ready, 1)
                    act.wait_ge(hid_ready, k + 1)
                    act.copy(hid_hi[i][:, :], hid[i][:, :]).then_inc(hid_hi_ready, 1)
                    if f < FT - 2:
                        split_w1(e, a, f + 2)
                    elif not final:
                        split_w1(e + a, 1 - a, f + 2 - FT)
                    if not (final and f == FT - 1):
                        split_w2(k + 1, (f + 1) % FT)
                    if f in (1, 2) and not (isinstance(u, int) and u == 0):
                        gate(u - 1, range(ST // 2 * (f - 1), ST // 2 * f))
                if final:
                    gate(u, range(ST))

        split_w1(0, 0, 0)
        split_w1(0, 0, 1)
        split_w2(0, 0)
        for k in range(KC):
            turned(0, 0, k)
        experts(act, body)

    @block.vector
    def _(dve):
        dve.wait_ge(b1_turned, 1)
        dve.tensor_scalar(b1_cols[:, :, :], tbank[0][:, 0:P].rearrange("p (e f) -> p e f", e=E), GELU_R, None, ALU.mult).then_inc(b1_ready, 1)
        dve.wait_ge(b1_ready, 1)

        def turned(u, a, k):
            dve.wait_ge(bxT_hi_ready, KC * u + k + 1)
            dve.tensor_tensor(xT_lo[a][:, k, :], tbank[k % 2][:, :], xT_hi[a][:, k, :].bitcast(F32), ALU.subtract).then_inc(t_emptied, 1)

        def split_w1(k, f):
            dve.wait_ge(w1_hi_ready, k + 1)
            dve.tensor_tensor(w1_lo[f % 2][:, :, :], w1_raw[:, :, f * P:(f + 1) * P], w1_hi[f % 2][:, :, :].bitcast(F32), ALU.subtract).then_inc(w1_lo_ready, 1)

        def split_w2(k, f):
            dve.wait_ge(w2_hi_ready, k + 1)
            dve.tensor_tensor(w2_lo[f % 2][:, :], w2_raw[:, f, :], w2_hi[f % 2][:, :].bitcast(F32), ALU.subtract).then_inc(w2_lo_ready, 1)

        def split_hid(k, f):
            dve.wait_ge(hid_hi_ready, k + 1)
            after(dve, y_filled, k - 1)
            dve.tensor_tensor(hid_lo[f % 2][:, :], hid[f % 2][:, :], hid_hi[f % 2][:, :].bitcast(F32), ALU.subtract).then_inc(hid_lo_ready, 1)

        def take_b1(e, half):
            cols = slice(half * FT // 2, (half + 1) * FT // 2)
            src = b1_cols[:, e, cols] if isinstance(e, int) else b1_cols[:, bass.ds(e, 1), cols].squeeze(1)
            dve.tensor_copy(b1_e[:, cols], src).then_inc(b1e_ready, 1)

        def body(e, last):
            for a in range(PASSES):
                u = PASSES * e + a
                final = last and a == PASSES - 1
                for f in range(FT):
                    k = FT * u + f
                    if TURN <= f - 1 < TURN + KC and not final:
                        turned(u + 1, 1 - a, f - 1 - TURN)
                    if f == 2 and a == 0:
                        after(dve, hid_ready, FT * u)
                        take_b1(e, 1)
                    if f == FT - 2 and a == 1 and not last:
                        dve.wait_ge(hid_ready, FT * u + FT // 2)
                        take_b1(e + 1, 0)
                    if f > 0:
                        split_hid(k, f)
                    if f < FT - 2 or not final:
                        split_w1(k + 2, (f + 2) % FT)
                    if f < FT - 1 or not final:
                        split_w2(k + 1, (f + 1) % FT)
                if not final:
                    split_hid(FT * (u + 1), 0)
                dve.wait_ge(b2_loaded, 16 * (e + 1))
                dve.wait_ge(y_filled, FT * (u + 1))
                after(dve, y_scaled, ST * u)
                for t in range(ST):
                    dve.scalar_tensor_tensor(y[:, t, :], ybank[t][:, :], 1.0 / GELU_R, b2_row[:, :], ALU.mult, ALU.add).then_inc(y_emptied, 1)

        split_w1(0, 0)
        split_w1(1, 1)
        split_w2(0, 0)
        for k in range(KC):
            turned(0, 0, k)
        take_b1(0, 0)
        split_hid(0, 0)
        experts(dve, body)


_ARGS = {
    "x": "L0_attn_x", "W_qkv": "L0_attn_W_qkv", "conv_w": "L0_attn_conv_w", "W_z": "L0_attn_W_z", "W_b": "L0_attn_W_b",
    "W_a": "L0_attn_W_a", "dt_bias": "L0_attn_dt_bias", "A_log": "L0_attn_A_log", "W_out": "L0_attn_W_out",
    "W_sw": "L0_ffn_W_sw", "b_sw": "L0_ffn_b_sw", "W1": "L0_ffn_W1", "b1": "L0_ffn_b1", "W2": "L0_ffn_W2", "b2": "L0_ffn_b2",
}


def kernel(**inputs):
    import numpy as _np
    import concourse.bacc as _bacc
    from concourse import mybir as _mybir
    from concourse.bass_utils import run_bass_kernel_spmd as _run

    nc = _bacc.Bacc("TRN2", target_bir_lowering=False, num_devices=1)
    arrays, args = {}, {}
    for name, given in _ARGS.items():
        a = _np.ascontiguousarray(inputs[given])
        arrays[f"in_{name}"] = a
        args[name] = nc.dram_tensor(f"in_{name}", a.shape, _mybir.dt.from_np(a.dtype), kind="ExternalInput").ap()
    shape = inputs["L0_attn_x"].shape
    out = nc.dram_tensor("out_0", shape, _mybir.dt.float32, kind="ExternalOutput").ap()
    build(nc, out=out, **args)
    r = _run(nc, [arrays], core_ids=[0])
    return r.results[0]["out_0"]
```
